# Optimizing a Trainium2 kernel written in Bass

```python
import numpy as np
import jax
import jax.numpy as jnp

def _softmax(x, axis=-1):
    return jax.nn.softmax(x, axis=axis)

def _gelu(x):
    return jax.nn.gelu(x, approximate=True)

def _silu(x):
    return jax.nn.silu(x)

def _sigmoid(x):
    return jax.nn.sigmoid(x)

def _layernorm(x, axis=-1, eps=1e-05):
    m = jnp.mean(x, axis=axis, keepdims=True)
    v = jnp.var(x, axis=axis, keepdims=True)
    return (x - m) / jnp.sqrt(v + eps)

def _scatter_add(tgt, idx, src, axis=0):
    return tgt.at[idx].add(src)

def _segment_sum(src, seg, n):
    return jax.ops.segment_sum(src, seg, n)
kernel_name = 'mk_adaln_ffn_d1_seqx_r2_2e9d1d'

def setup_inputs(seed: int=0):
    np.random.seed(seed)
    _w = jnp.asarray

    def _rec_inputs():
        import jax
        import jax.numpy as jnp
        _rk = jax.random.key(seed)
        x = -0.000125 + 0.9999 * jax.random.normal(jax.random.fold_in(_rk, 1), (8, 512, 2048), jnp.float32)
        _lenS = 512 - jax.random.randint(jax.random.fold_in(_rk, 7), (8,), 0, max(1, 512 // 4) + 1, jnp.int32)
        _lenS2 = 512 - jax.random.randint(jax.random.fold_in(_rk, 8), (8,), 0, max(1, 512 // 4) + 1, jnp.int32)
        itok_B_0_23 = jax.random.randint(jax.random.fold_in(_rk, 11), (8,), 0, 24, jnp.int32)
        return (x, itok_B_0_23)
    x, itok_B_0_23 = _rec_inputs()

    def _L0_cond_setup():
        import jax, jax.numpy as jnp
        import numpy as np
        R = 16
        ALPHA = 32
        SCALING = ALPHA / R
        SLOTS = 32
        IN_F = 2048
        OUT_F = 2048
        B, T = (8, 512)
        key = jax.random.key(seed)
        k1, k2, k3, k4, k5, k6 = jax.random.split(key, 6)
        x = jax.random.normal(k1, (B, T, IN_F), dtype=jnp.float32)
        adapter_mapping = jax.random.randint(k2, (B,), 0, SLOTS, dtype=jnp.int32)
        W = jax.random.normal(k3, (OUT_F, IN_F), dtype=jnp.float32) * 0.02
        b = jax.random.normal(k4, (OUT_F,), dtype=jnp.float32) * 0.02
        lora_As = jax.random.normal(k5, (SLOTS, IN_F, R), dtype=jnp.float32) * 0.02
        lora_Bs = jax.random.normal(k6, (SLOTS, R, OUT_F), dtype=jnp.float32) * 0.02
        return {'x': x, 'adapter_mapping': adapter_mapping, 'W': W, 'b': b, 'lora_As': lora_As, 'lora_Bs': lora_Bs}
    _L0_cond_all = _L0_cond_setup()
    _L0_cond_in = {k: v for k, v in _L0_cond_all.items() if k in ('W', 'b', 'lora_As', 'lora_Bs')}
    del _L0_cond_all

    def _L0_ffn_setup():
        import jax, jax.numpy as jnp
        import numpy as np
        R = 16
        LORA_ALPHA = 16
        SCALING = LORA_ALPHA / R
        key = jax.random.key(seed)
        kx, kr, ka = jax.random.split(key, 3)
        B, S, D, DO, E = (4, 1024, 2048, 2048, 8)
        x = jax.random.normal(kx, (B, S, D), dtype=jnp.float32)
        bound_r = 1.0 / np.sqrt(D)
        route_w = jax.random.uniform(kr, (E, D), jnp.float32, -bound_r, bound_r)
        bound_a = 1.0 / np.sqrt(D)
        A = jax.random.uniform(ka, (E, R, D), jnp.float32, -bound_a, bound_a)
        kb = jax.random.fold_in(key, 7)
        Bw = jax.random.normal(kb, (E, DO, R), dtype=jnp.float32) * 0.02
        return {'x': x, 'route_w': route_w, 'A': A, 'Bw': Bw}
    _L0_ffn_all = _L0_ffn_setup()
    _L0_ffn_in = {k: v for k, v in _L0_ffn_all.items() if k in ('route_w', 'A', 'Bw')}
    del _L0_ffn_all
    return {'x': x, 'itok_B_0_23': itok_B_0_23, 'L0_cond_W': _L0_cond_in['W'], 'L0_cond_b': _L0_cond_in['b'], 'L0_cond_lora_As': _L0_cond_in['lora_As'], 'L0_cond_lora_Bs': _L0_cond_in['lora_Bs'], 'L0_ffn_route_w': _L0_ffn_in['route_w'], 'L0_ffn_A': _L0_ffn_in['A'], 'L0_ffn_Bw': _L0_ffn_in['Bw']}

def reference(x, itok_B_0_23, L0_cond_W, L0_cond_b, L0_cond_lora_As, L0_cond_lora_Bs, L0_ffn_route_w, L0_ffn_A, L0_ffn_Bw):
    import jax
    import jax.numpy as jnp

    def _L0_cond_ref(x, adapter_mapping, W, b, lora_As, lora_Bs):
        import jax, jax.numpy as jnp
        import numpy as np
        R = 16
        ALPHA = 32
        SCALING = ALPHA / R
        SLOTS = 32
        IN_F = 2048
        OUT_F = 2048
        B, T = (8, 512)
        base_out = jnp.einsum('bti,oi->bto', x, W) + b
        A = lora_As[adapter_mapping]
        Bm = lora_Bs[adapter_mapping]
        lora_h = jnp.einsum('bti,bir->btr', x, A)
        lora_out = jnp.einsum('btr,bro->bto', lora_h, Bm)
        return base_out + lora_out * SCALING

    def _L0_ffn_ref(x, route_w, A, Bw):
        import jax, jax.numpy as jnp
        import numpy as np
        R = 16
        LORA_ALPHA = 16
        SCALING = LORA_ALPHA / R
        logits = jnp.einsum('bsd,ed->bse', x, route_w)
        topk_v, topk_idx = jax.lax.top_k(logits, 1)
        E = logits.shape[-1]
        route_weight = jax.nn.one_hot(topk_idx[..., 0], E, dtype=logits.dtype) * topk_v
        h = jnp.einsum('bsd,erd->bser', x, A)
        wh = route_weight[..., None] * h
        out = jnp.einsum('bser,eor->bso', wh, Bw) * SCALING
        return out
    x = x + _L0_ffn_ref(_L0_cond_ref(x, itok_B_0_23, L0_cond_W, L0_cond_b, L0_cond_lora_As, L0_cond_lora_Bs), L0_ffn_route_w, L0_ffn_A, L0_ffn_Bw)
    return x

_drawn_inputs = setup_inputs


def setup_inputs(seed=0):
    import zlib

    import numpy as np

    out = dict(_drawn_inputs(seed))
    spreads = {}
    factors = {'L0_cond_b': 8.0, 'L0_cond_lora_As': 4.418, 'L0_cond_lora_Bs': 4.377}
    for name, (base, spread) in spreads.items():
        noise = np.random.default_rng([zlib.crc32(name.encode()), seed]).standard_normal(out[name].shape)
        drawn = base * np.exp(spread * noise) if base else spread * noise
        out[name] = jnp.asarray(drawn.astype(out[name].dtype))
    for name, factor in factors.items():
        out[name] = (out[name] * factor).astype(out[name].dtype)
    return out
```

```python
from contextlib import ExitStack

import concourse.bass as bass
from concourse import mybir

ALU = mybir.AluOpType
ACT = mybir.ActivationFunctionType
AX_X = mybir.AxisListType.X
F32 = mybir.dt.float32
F32R = mybir.dt.float32r
I32 = mybir.dt.int32

P = 128
GROUP = 32
NGROUPS = P // GROUP


def adaln_ffn(nc, xT, slot_of, W, PT, bias, loraA, loraB, BwT, outT):
    NB, NQ, _, PC, T = xT.shape
    C = NQ * PC
    NP2 = C // 2
    NWB, NWH, _, WO, WI = W.shape
    E = 8
    R = 16
    ER = E * R
    PN = ER + E
    SCALING = 32 / R
    NSLOTS = loraA.shape[0]
    TQ = T // P
    BIAS_ROW = E + R
    XRING = 12
    WRING = 8
    NPT = 4
    SRING = 4
    NWP = NWB * NWH
    NPIECES = NB * NQ
    assert ER == P and WI == 2 * P and NWB == NP2 and NB * R == P and BIAS_ROW < GROUP

    ctx = ExitStack()
    with ctx:
        def sb(name, shape, dt=F32, scope=ctx):
            return scope.enter_context(nc.sbuf_tensor(name, shape, dt))

        def psum(name, shape):
            return ctx.enter_context(nc.psum_tensor(name, shape, F32))

        def sem(name):
            return ctx.enter_context(nc.semaphore(name))

        phase1 = ExitStack()
        w_ring = sb("w_ring", [P, WRING, WO, WI], F32, phase1)
        phase1.close()
        x_hi = sb("x_hi", [P, SRING, 2, T], F32R)
        x_lo = sb("x_lo", [P, SRING, 2, T], F32R)
        assert WRING == 2 * SRING and WO * WI == 2 * T

        x_ring = sb("x_ring", [P, XRING, PC, T])
        lb = x_ring[:, 8, :, :].rearrange("p c t -> p (c t)").rearrange("p (b c r) -> p b c r", b=NB, c=C)
        bw_raw = x_ring[:, 9, :, :].rearrange("p c t -> p (c t)")
        place = x_ring[:, 10, 0:2, :].rearrange("p c t -> p (c t)").rearrange("p (b g j) -> p b g j", b=NB, g=NGROUPS)
        lb_cols = x_ring[:, 11, :, :].rearrange("p c t -> p (c t)").rearrange("p (c b r) -> p c b r", b=NB, c=C)
        EARLY = range(8, 12)

        phase1 = ExitStack()
        pt = sb("pt", [P, C, PN], F32, phase1)
        g_a = sb("g_a", [P, NB, ER], F32, phase1)
        bp = sb("bp", [P, PN], F32, phase1)
        gz = sb("gz", [P, PN], F32, phase1)
        phase1.close()
        e_hi = sb("e_hi", [P, T], F32R)
        e_lo = sb("e_lo", [P, T], F32R)
        wh_hi = [sb(f"wh_hi{i}", [P, T], F32R) for i in range(2)]
        wh_lo = [sb(f"wh_lo{i}", [P, T], F32R) for i in range(2)]
        route = sb("route", [P, TQ, E, R])
        assert C * PN + NB * ER + 2 * PN <= 6 * T + TQ * ER, "the second lot covers the first"

        pb_sum = [sb(f"pb_sum{i}", [P, PN]) for i in range(2)]
        bias_sb = sb("bias_sb", [P, C])
        warm = sb("warm", [P, T], mybir.dt.bfloat16)
        m_hi = sb("m_hi", [P, C, ER], F32R)
        m_lo = sb("m_lo", [P, C, ER], F32R)
        ext = [sb(f"ext{i}", [P, C, GROUP]) for i in range(2)]
        la = sb("la", [P, NB, C, R])
        bw_hi = sb("bw_hi", [P, C * P], F32R)
        bw_lo = sb("bw_lo", [P, C * P], F32R)
        g_hi = sb("g_hi", [P, NB, ER], F32R)
        g_lo = sb("g_lo", [P, NB, ER], F32R)
        g_route = sb("g_route", [P, NB, GROUP])
        ones = sb("ones", [P, 1])
        z = sb("z", [E + 1, PN])
        place_z = sb("place_z", [E + 1, NGROUPS, GROUP])
        e_bias = sb("e_bias", [P, 1])
        ident = sb("ident", [P, P])
        slots = sb("slots", [1, NB], I32)
        prefer = sb("prefer", [P, E])
        e_sb = sb("e_sb", [P, T])
        logt_sb = sb("logt_sb", [P, P])
        h_sb = sb("h_sb", [P, T])
        top = sb("top", [P, TQ])
        is_top = sb("is_top", [P, TQ, E])
        score = sb("score", [P, TQ, E])
        best = sb("best", [P, TQ])
        one_hot = sb("one_hot", [P, TQ, E])

        bank_e = psum("bank_e", [P, T])
        bank_h = psum("bank_h", [P, T])
        bank_r = psum("bank_r", [P, T])
        bank_l = psum("bank_l", [P, T])
        bank_out = [psum(f"bank_out{i}", [P, 2, T]) for i in range(2)]
        logits = bank_l[:, P:2 * P].rearrange("p (q j) -> p q j", j=GROUP)[:, :, 0:E]
        g_banks = [(bank_e, 0, 3), (bank_h, 3, 6), (bank_r, 6, NB)]

        d_slots, d_bias, d_bw, d_lb, d_la0, d_la = (sem(n) for n in ("d_slots", "d_bias", "d_bw", "d_lb", "d_la0", "d_la"))
        d_pt = [sem(f"d_pt{i}") for i in range(NPT)]
        d_w = [sem(f"d_w{i}") for i in range(WRING)]
        d_x = [sem(f"d_x{i}") for i in range(XRING)]
        d_out = [sem(f"d_out{i}") for i in range(XRING)]
        d_last = sem("d_last")
        g_zero, g_const, g_lb, g_ext = sem("g_zero"), sem("g_const"), sem("g_lb"), sem("g_ext")
        t_pb, t_bp, t_gz, t_g, t_w = (sem(n) for n in ("t_pb", "t_bp", "t_gz", "t_g", "t_w"))
        t_ext, t_main, t_logt, t_log, t_h, t_route, t_out = (sem(n) for n in ("t_ext", "t_main", "t_logt", "t_log", "t_h", "t_route", "t_out"))
        a_pb, a_bp, a_gz, a_ghi, a_bw, a_m = (sem(n) for n in ("a_pb", "a_bp", "a_gz", "a_ghi", "a_bw", "a_m"))
        a_xhi, a_e, a_ehi, a_log, a_h, a_wh = (sem(n) for n in ("a_xhi", "a_e", "a_ehi", "a_log", "a_h", "a_wh"))
        v_warm, v_pb, v_g, v_glo, v_elo, v_bw, v_m, v_xlo, v_top, v_route, v_wh, v_whlo, v_out = (
            sem(n) for n in ("v_warm", "v_pb", "v_g", "v_glo", "v_elo", "v_bw", "v_m", "v_xlo", "v_top", "v_route", "v_wh", "v_whlo", "v_out"))

        UNITS = [(b, 0, T) for b in range(NB - 1)] + [(NB - 1, t, T // 2) for t in (0, T // 2)]
        NU = len(UNITS)
        HELD = [2] * (NU - 1) + [3]

        def x_landed(eng, k):
            eng.wait_ge(d_x[k % XRING], 16 * (k // XRING + 1))

        def x_pair(u, j):
            b, t0, nt = UNITS[u]
            k = NQ * b + 2 * j // PC
            return x_ring[:, k % XRING, 2 * j % PC:2 * j % PC + 2, t0:t0 + nt]

        CONSTS = E + 7
        WARM_UP = 9
        BW_AT = 19
        BP_AT, G_AT = 20, 24
        CHOOSE_AT, EHI_AT, ELO_AT = 1, 5, 3

        def out_banks(u, j):
            nt = UNITS[u][2]
            if nt == T:
                return bank_out[j % 2][:, :, :]
            return bank_out[j // 2 % 2][:, j % 2, :].rearrange("p (i t) -> p i t", i=2)

        def pairs_added(u, j):
            if UNITS[u][2] == T:
                return NP2 * u + j - 1
            if UNITS[u - 1][2] == T and j < 4:
                return NP2 * u - 1 + j // 2
            return NP2 * u + j - 3

        block = ctx.enter_context(nc.Block())

        @block.sync
        def _(sp):
            def load_w(n):
                if n >= WRING:
                    sp.wait_ge(t_w, n - WRING + 1)
                sp.dma_start(w_ring[:, n % WRING, :, :], W[n // NWH, n % NWH]).then_inc(d_w[n % WRING], 16)

            def load_x(k):
                slot = k % XRING
                if k >= XRING:
                    sp.wait_ge(d_out[slot], 16 * (k // XRING))
                elif slot in EARLY:
                    sp.wait_ge(t_g, len(g_banks))
                    sp.wait_ge(v_bw, 1)
                sp.dma_start(x_ring[:, slot, :, :], xT[k // NQ, k % NQ]).then_inc(d_x[slot], 16)

            def store(k):
                sp.wait_ge(v_out, (k + 1) * (PC // 2))
                sp.dma_start(outT[k // NQ, k % NQ], x_ring[:, k % XRING, :, :]).then_inc(d_out[k % XRING], 16)

            for n in range(NWP):
                if n < NPT:
                    part = slice(n * C // NPT, (n + 1) * C // NPT)
                    sp.dma_start(pt[:, part, :], PT[:, part, :]).then_inc(d_pt[n], 16)
                load_w(n)
                if n == NPT:
                    sp.dma_start(bias_sb[:, :], bias).then_inc(d_bias, 16)
                if n == BW_AT:
                    sp.dma_start(bw_raw, BwT).then_inc(d_bw, 16)
                if n >= NWP - 4 * NQ and n % 4 == 3:
                    load_x((n - NWP + 4 * NQ) // 4)
            for k in range(NQ, XRING):
                load_x(k)
            LAG = 2
            LAST = NPIECES - NQ
            for k in range(LAST):
                store(k)
                if k >= LAG and k - LAG + XRING < NPIECES:
                    load_x(k - LAG + XRING)
            for u in range(NB - 1, NU):
                b, t0, nt = UNITS[u]
                for j in range(NP2):
                    sp.wait_ge(v_out, NP2 * u + j + 1)
                    q, c = 2 * j // PC, 2 * j % PC
                    sp.dma_start(outT[b, q, :, c:c + 2, t0:t0 + nt], x_pair(u, j)).then_inc(d_last, 16)
            for s in range(XRING):
                sp.wait_ge(d_out[s], 16 * len(range(s, LAST, XRING)))
            sp.wait_ge(d_last, 16 * NP2 * (NU - NB + 1))

        @block.gpsimd
        def _(pool):
            zeroed = (place, place_z[:, :, :], z[:, :], e_bias[:, :], g_route[:, :, :], ident[:, :],
                      ext[0][:, :, :], ext[1][:, :, :])
            for t in zeroed:
                pool.memset(t, 0.0).then_inc(g_zero, 1)
            pool.memset(ones[:, :], 1.0).then_inc(g_const, 1)
            for e in range(E):
                pool.memset(prefer[:, e:e + 1], float(E - e)).then_inc(g_const, 1)
            pool.wait_ge(g_zero, len(zeroed))

            def where_zero(ap, value, base, pattern):
                pool.affine_select(out=ap, in_=ap, compare_op=ALU.not_equal, fill=value, base=base,
                                   pattern=pattern, channel_multiplier=1).then_inc(g_const, 1)

            where_zero(place[:, :, :, E:E + R], SCALING, 0, [[-R, NB], [0, NGROUPS], [-1, R]])
            where_zero(place_z[:, :, 0:E], 1.0, -1, [[0, NGROUPS], [-1, E]])
            where_zero(place_z[:, 0, BIAS_ROW:BIAS_ROW + 1], 1.0, 0, [[0, 1]])
            where_zero(z[:, ER:PN], 1.0, -1, [[-1, E]])
            where_zero(e_bias[:, :], 1.0, -BIAS_ROW, [[0, 1]])
            where_zero(ident[:, :], 1.0, 0, [[-1, P]])
            pool.wait_ge(d_lb, 16 * NB)
            pool.tensor_copy(lb_cols, lb.rearrange("p b c r -> p c b r")).then_inc(g_lb, 1)
            pool.wait_ge(d_la0, 16 * 2)
            for u, (b, _, _) in enumerate(UNITS):
                if u == 2:
                    pool.wait_ge(d_la, 16 * (NB - 2))
                if u >= 2:
                    pool.wait_ge(t_ext, u - 1)
                pool.tensor_copy(ext[u % 2][:, :, E:E + R], la[:, b, :, :]).then_inc(g_ext, 1)


        @block.scalar
        def _(act):
            act.dma_start(slots[:, :], slot_of).then_inc(d_slots, 16)
            act.wait_ge(d_slots, 16)
            slot = [act.value_load(slots[0:1, b:b + 1], min_val=0, max_val=NSLOTS - 1) for b in range(NB)]

            def load_a(b0, b1):
                for b in range(b0, b1):
                    act.dma_start(la[:, b, :, :].rearrange("p c r -> p (c r)"),
                                  loraA[bass.ds(slot[b], 1), :, :].rearrange("s p n -> p (s n)")).then_inc(
                                      d_la0 if b < 2 else d_la, 16)

            def copy(out, in_, done):
                act.activation(out, in_, ACT.Copy).then_inc(done, 1)

            def m_block(n):
                act.wait_ge(t_w, NWH * (n + 1))
                copy(m_hi[:, 2 * n:2 * n + 2, :], bank_out[n % 2][:, :, 0:ER], a_m)
                for i in range(2):
                    copy(ext[i][:, 2 * n:2 * n + 2, 0:E], bank_out[n % 2][:, :, ER:PN], a_m)

            act.wait_ge(g_const, CONSTS)
            for n in range(NWB):
                if n == 1:
                    for b in range(NB):
                        act.dma_start(lb[:, b, :, :].rearrange("p c r -> p (c r)"),
                                      loraB[bass.ds(slot[b], 1), :, :].rearrange("s p n -> p (s n)")).then_inc(d_lb, 16)
                    load_a(0, 2)
                if n == BP_AT // NWH:
                    act.wait_ge(t_bp, 1)
                    copy(bp[:, :], bank_l[:, 0:PN], a_bp)
                    act.wait_ge(t_pb, 1)
                    copy(z[0:1, :], bank_r[0:1, 0:PN], a_pb)
                if n == G_AT // NWH:
                    load_a(2, NB)
                    act.wait_ge(t_gz, 1)
                    copy(gz[:, :], bank_l[:, 0:PN], a_gz)
                if n == NWB - 1:
                    act.wait_ge(v_g, 2 * len(g_banks))
                    copy(g_hi[:, :, :], g_a[:, :, :], a_ghi)
                if n == NWB - 2:
                    act.wait_ge(d_bw, 16)
                    copy(bw_hi[:, :], bw_raw, a_bw)
                m_block(n)

            def split_hi(u, j):
                b, _, nt = UNITS[u]
                g = NP2 * u + j
                if u == 0 and j < SRING:
                    act.wait_ge(t_w, NWP - WRING + j + 1)
                elif g >= SRING:
                    act.wait_ge(t_main, g - SRING + 1)
                x_landed(act, NQ * b + 2 * j // PC)
                copy(x_hi[:, g % SRING, :, 0:nt], x_pair(u, j), a_xhi)

            for j in range(SRING):
                split_hi(0, j)
            for u, (b, _, nt) in enumerate(UNITS):
                act.wait_ge(t_ext, u + 1)
                act.activation(e_sb[:, 0:nt], bank_e[:, 0:nt], ACT.Identity, bias=e_bias[:, 0:1]).then_inc(a_e, 1)
                for j in range(SRING, NP2):
                    split_hi(u, j)
                    if j == SRING:
                        act.wait_ge(t_logt, u + 1)
                        copy(logt_sb[0:nt // P * GROUP, :], bank_l[0:nt // P * GROUP, 0:P], a_log)
                    if j == EHI_AT:
                        act.wait_ge(a_e, u + 1)
                        if u >= 1:
                            act.wait_ge(t_h, u)
                        copy(e_hi[:, 0:nt], e_sb[:, 0:nt], a_ehi)
                if u + 1 < NU:
                    for j in range(SRING):
                        split_hi(u + 1, j)
                act.wait_ge(t_h, u + 1)
                if u >= 1:
                    act.wait_ge(v_whlo, u)
                copy(h_sb[:, 0:nt], bank_h[:, 0:nt], a_h)
                act.wait_ge(v_wh, u + 1)
                if u >= 2:
                    act.wait_ge(t_out, NP2 * (u - 1))
                copy(wh_hi[u % 2][:, 0:nt], h_sb[:, 0:nt], a_wh)

        @block.vector
        def _(dve):
            def sub(out, a, b, done):
                dve.tensor_tensor(out, a, b, ALU.subtract).then_inc(done, 1)

            def m_block(n):
                dve.wait_ge(a_m, 3 * (n + 1))
                sub(m_lo[:, 2 * n:2 * n + 2, :], bank_out[n % 2][:, :, 0:ER], m_hi[:, 2 * n:2 * n + 2, :], v_m)

            dve.memset(warm[:, :], 0.0).then_inc(v_warm, 1)
            dve.wait_ge(d_bias, 16)
            for c in range(C):
                if c % (C // NPT) == 0:
                    dve.wait_ge(d_pt[c // (C // NPT)], 16)
                if c == 0:
                    dve.tensor_scalar(pb_sum[0][:, :], pt[:, 0, :], bias_sb[:, 0:1], None, ALU.mult).then_inc(v_pb, 1)
                else:
                    dve.wait_ge(v_pb, c)
                    dve.scalar_tensor_tensor(out=pb_sum[c % 2][:, :], in0=pt[:, c, :], scalar=bias_sb[:, c:c + 1],
                                             in1=pb_sum[(c - 1) % 2][:, :], op0=ALU.mult, op1=ALU.add).then_inc(v_pb, 1)
            for n in range(NWB):
                if n == G_AT // NWH:
                    dve.wait_ge(a_gz, 1)
                    for i, (bank, b0, b1) in enumerate(g_banks):
                        dve.wait_ge(t_g, i + 1)
                        sums = bank[:, 0:(b1 - b0) * PN].rearrange("p (b n) -> p b n", n=PN)
                        for out, cut in ((g_a[:, b0:b1, :], slice(0, ER)), (g_route[:, b0:b1, 0:E], slice(ER, PN))):
                            shared = gz[:, cut].unsqueeze(1).broadcast_to([P, b1 - b0, cut.stop - cut.start])
                            dve.tensor_tensor(out, sums[:, :, cut], shared, ALU.add).then_inc(v_g, 1)
                if n == NWB - 1:
                    dve.wait_ge(a_ghi, 1)
                    sub(g_lo[:, :, :], g_a[:, :, :], g_hi[:, :, :], v_glo)
                if n == NWB - 2:
                    dve.wait_ge(a_bw, 1)
                    sub(bw_lo[:, :], bw_raw, bw_hi[:, :], v_bw)
                m_block(n)

            def split_lo(u, j):
                nt = UNITS[u][2]
                g = NP2 * u + j
                if u == 0 and j < SRING:
                    dve.wait_ge(t_w, NWP - SRING + j + 1)
                elif g >= SRING:
                    dve.wait_ge(t_main, g - SRING + 1)
                dve.wait_ge(a_xhi, g + 1)
                sub(x_lo[:, g % SRING, :, 0:nt], x_pair(u, j), x_hi[:, g % SRING, :, 0:nt], v_xlo)

            def choose(u):
                q = UNITS[u][2] // P
                over_e = lambda ap: ap.unsqueeze(2).broadcast_to([P, q, E])
                over_r = lambda ap: ap.unsqueeze(3).broadcast_to([P, q, E, R])
                seen = logits[:, 0:q, :]
                dve.wait_ge(t_log, u + 1)
                n = 5 * u
                dve.tensor_reduce(top[:, 0:q], seen, AX_X, ALU.max).then_inc(v_top, 1)
                dve.wait_ge(v_top, n + 1)
                dve.tensor_tensor(is_top[:, 0:q, :], seen, over_e(top[:, 0:q]), ALU.is_ge).then_inc(v_top, 1)
                dve.wait_ge(v_top, n + 2)
                dve.tensor_tensor(score[:, 0:q, :], is_top[:, 0:q, :], prefer[:, :].unsqueeze(1).broadcast_to([P, q, E]),
                                  ALU.mult).then_inc(v_top, 1)
                dve.wait_ge(v_top, n + 3)
                dve.tensor_reduce(best[:, 0:q], score[:, 0:q, :], AX_X, ALU.max).then_inc(v_top, 1)
                dve.wait_ge(v_top, n + 4)
                dve.tensor_tensor(one_hot[:, 0:q, :], score[:, 0:q, :], over_e(best[:, 0:q]), ALU.is_equal).then_inc(v_top, 1)
                dve.wait_ge(v_top, n + 5)
                if u >= 1:
                    dve.wait_ge(t_route, u)
                dve.tensor_tensor(route[:, 0:q, :, :], over_r(one_hot[:, 0:q, :]), over_r(over_e(top[:, 0:q])),
                                  ALU.mult).then_inc(v_route, 1)

            def weigh(u):
                nt = UNITS[u][2]
                dve.wait_ge(a_h, u + 1)
                dve.wait_ge(t_route, u + 1)
                dve.tensor_tensor(h_sb[:, 0:nt], h_sb[:, 0:nt], bank_r[:, 0:nt], ALU.mult).then_inc(v_wh, 1)

            def weigh_lo(u):
                nt = UNITS[u][2]
                dve.wait_ge(a_wh, u + 1)
                sub(wh_lo[u % 2][:, 0:nt], h_sb[:, 0:nt], wh_hi[u % 2][:, 0:nt], v_whlo)

            def add_x(u, j):
                x = x_pair(u, j)
                dve.wait_ge(t_out, NP2 * u + j + 1)
                dve.tensor_tensor(x, out_banks(u, j), x, ALU.add).then_inc(v_out, 1)

            dve.wait_ge(g_const, CONSTS)
            for j in range(SRING):
                split_lo(0, j)
            for u in range(NU):
                for j in range(NP2):
                    if j < SRING:
                        split_lo(u, SRING + j)
                    elif u + 1 < NU:
                        split_lo(u + 1, j - SRING)
                    if u >= 1 and 1 <= j <= NP2 - HELD[u]:
                        add_x(u - 1, j - 1)
                    if j == CHOOSE_AT:
                        choose(u)
                    if j == ELO_AT:
                        dve.wait_ge(a_ehi, u + 1)
                        sub(e_lo[:, 0:UNITS[u][2]], e_sb[:, 0:UNITS[u][2]], e_hi[:, 0:UNITS[u][2]], v_elo)
                weigh(u)
                if u >= 1:
                    add_x(u - 1, NP2 - HELD[u])
                weigh_lo(u)
                if u >= 1:
                    for j in range(NP2 - HELD[u] + 1, NP2):
                        add_x(u - 1, j)
            for j in range(NP2):
                add_x(NU - 1, j)

        @block.tensor
        def _(pe):
            mm = pe.matmul

            def w_piece(n):
                blk, half = divmod(n, NWH)
                pe.wait_ge(d_w[n % WRING], 16 * (n // WRING + 1))
                if half == 0 and blk >= 2:
                    pe.wait_ge(v_m, blk - 1)
                for i in range(2):
                    for o in range(WO):
                        k = half * WO + o
                        if blk == 0 and i == 0 and k % (C // NPT) == 0:
                            pe.wait_ge(d_pt[k // (C // NPT)], 16)
                        last = mm(bank_out[blk % 2][:, i, 0:PN], w_ring[:, n % WRING, o, i * P:(i + 1) * P],
                                  pt[:, k, :], start=(k == 0), stop=(k == C - 1))
                last.then_inc(t_w, 1)

            pe.wait_ge(v_warm, 1)
            for _ in range(WARM_UP):
                mm(bank_h[:, :], warm[:, 0:P], warm[:, :], start=True, stop=True)
            for n in range(BP_AT):
                w_piece(n)
            pe.wait_ge(g_lb, 1)
            for c in range(C):
                last = mm(bank_l[:, 0:PN], lb_cols[:, c, :, :].rearrange("p b r -> p (b r)"), pt[:, c, :],
                          start=(c == 0), stop=(c == C - 1))
            last.then_inc(t_bp, 1)
            pe.wait_ge(v_pb, C)
            pe.wait_ge(g_const, CONSTS)
            mm(bank_r[0:1, 0:PN], ones[:, :], pb_sum[(C - 1) % 2][:, :], start=True, stop=True).then_inc(t_pb, 1)
            for n in range(BP_AT, G_AT):
                w_piece(n)
            pe.wait_ge(a_bp, 1)
            pe.wait_ge(a_pb, 1)
            mm(bank_l[:, 0:PN], place_z[:, :, :], z[:, :], start=True, stop=True).then_inc(t_gz, 1)
            for bank, b0, b1 in g_banks:
                for b in range(b0, b1):
                    last = mm(bank[:, (b - b0) * PN:(b - b0 + 1) * PN], place[:, b, :, :], bp[:, :], start=True, stop=True)
                last.then_inc(t_g, 1)
            for n in range(G_AT, NWP):
                w_piece(n)

            def out_pair(u, j):
                nt = UNITS[u][2]
                if u == 0 and j < 2:
                    pe.wait_ge(v_m, NWB)
                else:
                    pe.wait_ge(v_out, pairs_added(u, j))
                if u == 0 and j == 0:
                    pe.wait_ge(v_bw, 1)
                if j == 0:
                    pe.wait_ge(v_whlo, u + 1)
                hi, lo = wh_hi[u % 2][:, 0:nt], wh_lo[u % 2][:, 0:nt]
                for i in range(2):
                    o = slice((2 * j + i) * P, (2 * j + i + 1) * P)
                    out = out_banks(u, j)[:, i, :]
                    mm(out, bw_hi[:, o], hi, start=True, stop=False)
                    mm(out, bw_hi[:, o], lo, start=False, stop=False)
                    last = mm(out, bw_lo[:, o], hi, start=False, stop=True)
                last.then_inc(t_out, 1)

            pe.wait_ge(v_glo, 1)
            for u, (b, _, nt) in enumerate(UNITS):
                pe.wait_ge(g_ext, u + 1)
                if u >= 1:
                    pe.wait_ge(a_e, u)
                for r in range(C // NGROUPS):
                    for g in range(NGROUPS):
                        c = r * NGROUPS + g
                        if c % PC == 0:
                            x_landed(pe, NQ * b + c // PC)
                        if u == 0 and c % 2 == 0:
                            pe.wait_ge(a_m, 3 * (c // 2 + 1))
                        last = mm(bank_e[g * GROUP:(g + 1) * GROUP, 0:nt], ext[u % 2][:, c, :], x_pair(u, c // 2)[:, c % 2, :],
                                  start=(r == 0), stop=(r == C // NGROUPS - 1))
                last.then_inc(t_ext, 1)
                if u >= 1:
                    pe.wait_ge(a_h, u)
                else:
                    pe.wait_ge(v_m, NWB)
                h = bank_h[:, 0:nt]
                for j in range(NP2):
                    g = NP2 * u + j
                    pe.wait_ge(v_xlo, g + 1)
                    for i in range(2):
                        c = 2 * j + i
                        hi, lo = x_hi[:, g % SRING, i, 0:nt], x_lo[:, g % SRING, i, 0:nt]
                        mm(h, m_hi[:, c, :], hi, start=(c == 0), stop=False)
                        mm(h, m_hi[:, c, :], lo, start=False, stop=False)
                        last = mm(h, m_lo[:, c, :], hi, start=False, stop=False)
                    last.then_inc(t_main, 1)
                    if j == 0:
                        pe.wait_ge(a_e, u + 1)
                        if u >= 1:
                            pe.wait_ge(v_top, 5 * u)
                        for q in range(nt // P):
                            last = mm(bank_l[q * GROUP:(q + 1) * GROUP, 0:P], g_route[:, b, :],
                                      e_sb[:, q * P:(q + 1) * P], start=True, stop=True)
                        last.then_inc(t_logt, 1)
                    if j == 1:
                        rows = nt // P * GROUP
                        pe.wait_ge(a_log, u + 1)
                        pe.transpose(bank_l[:, P:P + rows], logt_sb[0:rows, :], ident[0:rows, 0:rows]).then_inc(t_log, 1)
                    if u >= 1 and 1 <= j <= NP2 - HELD[u]:
                        out_pair(u - 1, j - 1)
                pe.wait_ge(v_elo, u + 1)
                mm(h, g_hi[:, b, :], e_hi[:, 0:nt], start=False, stop=False)
                mm(h, g_hi[:, b, :], e_lo[:, 0:nt], start=False, stop=False)
                mm(h, g_lo[:, b, :], e_hi[:, 0:nt], start=False, stop=True).then_inc(t_h, 1)
                pe.wait_ge(v_route, u + 1)
                if u >= 1:
                    pe.wait_ge(v_wh, u)
                for q in range(nt // P):
                    last = pe.transpose(bank_r[:, q * P:(q + 1) * P], route[:, q, :, :].rearrange("p e r -> p (e r)"),
                                        ident[:, :])
                last.then_inc(t_route, 1)
                if u >= 1:
                    for j in range(NP2 - HELD[u], NP2):
                        out_pair(u - 1, j)
            for j in range(NP2):
                out_pair(NU - 1, j)


def kernel(x, itok_B_0_23, L0_cond_W, L0_cond_b, L0_cond_lora_As, L0_cond_lora_Bs, L0_ffn_route_w, L0_ffn_A, L0_ffn_Bw):
    import numpy as np
    import concourse.bacc as bacc
    from concourse.bass_utils import run_bass_kernel_spmd

    x, slot_of, W, bias, loraA, loraB, route_w, A, Bw = (np.asarray(a) for a in (
        x, itok_B_0_23, L0_cond_W, L0_cond_b, L0_cond_lora_As, L0_cond_lora_Bs, L0_ffn_route_w, L0_ffn_A, L0_ffn_Bw))
    nb, t, d = x.shape
    dout, din = W.shape
    nslots, _, r = loraA.shape
    e = route_w.shape[0]
    c, pc, wblock, wo = d // P, 4, 2 * P, 4
    arrays = {
        "xT": x.reshape(nb, t, c // pc, pc, P).transpose(0, 2, 4, 3, 1),
        "slot_of": slot_of.reshape(1, nb),
        "W": W.reshape(dout // (wo * P), wo, P, din // wblock, wblock).transpose(3, 0, 2, 1, 4),
        "PT": np.concatenate([A.reshape(e * r, dout), route_w]).reshape(e * r + e, dout // P, P).transpose(2, 1, 0),
        "bias": bias.reshape(dout // P, P).T,
        "loraA": loraA.reshape(nslots, c, P, r).transpose(0, 2, 1, 3).reshape(nslots, P, c * r),
        "loraB": loraB.reshape(nslots, r, dout // P, P).transpose(0, 3, 2, 1).reshape(nslots, P, dout // P * r),
        "BwT": Bw.transpose(0, 2, 1).reshape(e * r, dout),
    }
    arrays = {name: np.ascontiguousarray(a) for name, a in arrays.items()}
    nc = bacc.Bacc("TRN2", target_bir_lowering=False, num_devices=1)
    ins = [nc.dram_tensor(name, a.shape, mybir.dt.from_np(a.dtype), kind="ExternalInput").ap() for name, a in arrays.items()]
    outT = nc.dram_tensor("outT", arrays["xT"].shape, F32, kind="ExternalOutput").ap()
    adaln_ffn(nc, *ins, outT)
    got = run_bass_kernel_spmd(nc, [arrays], core_ids=[0]).results[0]["outT"]
    return np.ascontiguousarray(got.transpose(0, 4, 1, 3, 2).reshape(nb, t, d))
```
